# Optimizing a Trainium2 kernel written in Bass

```python
import numpy as np
import jax
import jax.numpy as jnp

def _softmax(x, axis=-1):
    return jax.nn.softmax(x, axis=axis)

def _gelu(x):
    return jax.nn.gelu(x, approximate=True)

def _silu(x):
    return jax.nn.silu(x)

def _sigmoid(x):
    return jax.nn.sigmoid(x)

def _layernorm(x, axis=-1, eps=1e-05):
    m = jnp.mean(x, axis=axis, keepdims=True)
    v = jnp.var(x, axis=axis, keepdims=True)
    return (x - m) / jnp.sqrt(v + eps)

def _scatter_add(tgt, idx, src, axis=0):
    return tgt.at[idx].add(src)

def _segment_sum(src, seg, n):
    return jax.ops.segment_sum(src, seg, n)
kernel_name = 'mk_gnn_ffn_d1_gnn_r16_ef57d3'

def setup_inputs(seed: int=0):
    np.random.seed(seed)
    _w = jnp.asarray

    def _rec_inputs():
        import jax
        import jax.numpy as jnp
        _gk = jax.random.key(seed)
        x = -0.0003713 + 1 * jax.random.normal(jax.random.fold_in(_gk, 1), (3125, 256), jnp.float32)
        _s = jax.random.randint(jax.random.fold_in(_gk, 2), (25000,), 0, 3125, jnp.int32)
        _d = jax.random.randint(jax.random.fold_in(_gk, 3), (25000,), 0, 3125, jnp.int32)
        _loop = jnp.arange(3125, dtype=jnp.int32)
        src = jnp.concatenate([_s, _d, _loop])
        dst = jnp.concatenate([_d, _s, _loop])
        _o = jnp.argsort(dst, stable=True)
        src = src[_o]
        dst = dst[_o]
        edge_type_8 = jax.random.randint(jax.random.fold_in(_gk, 12), (53125,), 0, 8, jnp.int32)
        return (x, src, dst, edge_type_8)
    x, src, dst, edge_type_8 = _rec_inputs()

    def _L0_gnn_setup():
        import jax, jax.numpy as jnp
        import numpy as np
        NUM_NODES = 3125
        NUM_EDGES = 50000
        IN_DIM = 256
        OUT_DIM = 256
        NUM_RELATIONS = 8
        key = jax.random.key(seed)
        k1, k2, k3, k4 = jax.random.split(key, 4)
        node_repr = jax.random.normal(k1, (NUM_NODES, IN_DIM), dtype=jnp.float32)
        edge_index = jax.random.randint(k2, (2, NUM_EDGES), 0, NUM_NODES, dtype=jnp.int64)
        edge_types = jax.random.randint(k3, (NUM_EDGES,), 0, NUM_RELATIONS, dtype=jnp.int64)
        limit = float(np.sqrt(6.0 / (IN_DIM + OUT_DIM)))
        weight = jax.random.uniform(k4, (NUM_RELATIONS, OUT_DIM, IN_DIM), dtype=jnp.float32, minval=-limit, maxval=limit)
        bias = jnp.zeros((OUT_DIM,), dtype=jnp.float32)
        return {'node_repr': node_repr, 'weight': weight, 'bias': bias, 'edge_index': edge_index, 'edge_types': edge_types}
    _L0_gnn_all = _L0_gnn_setup()
    _L0_gnn_in = {k: v for k, v in _L0_gnn_all.items() if k in ('weight', 'bias')}
    del _L0_gnn_all

    def _L0_ffn_setup():
        import jax, jax.numpy as jnp
        import numpy as np
        D_MODEL = 256
        N_EXPERTS = 16
        HIDDEN = 512
        SCALE = 0.02
        key = jax.random.key(seed)
        ks = jax.random.split(key, 5)
        x = jax.random.normal(ks[0], (4, 512, D_MODEL), dtype=jnp.float32)
        gate_w = jax.random.normal(ks[1], (D_MODEL, N_EXPERTS), dtype=jnp.float32) * SCALE
        gate_b = jnp.zeros((N_EXPERTS,), dtype=jnp.float32)
        w1 = jax.random.normal(ks[2], (N_EXPERTS, D_MODEL, HIDDEN), dtype=jnp.float32) * SCALE
        w2 = jax.random.normal(ks[3], (N_EXPERTS, D_MODEL, HIDDEN), dtype=jnp.float32) * SCALE
        w3 = jax.random.normal(ks[4], (N_EXPERTS, HIDDEN, D_MODEL), dtype=jnp.float32) * SCALE
        return {'x': x, 'gate_w': gate_w, 'gate_b': gate_b, 'w1': w1, 'w2': w2, 'w3': w3}
    _L0_ffn_all = _L0_ffn_setup()
    _L0_ffn_in = {k: v for k, v in _L0_ffn_all.items() if k in ('gate_w', 'gate_b', 'w1', 'w2', 'w3')}
    del _L0_ffn_all
    return {'x': x, 'src': src, 'dst': dst, 'edge_type_8': edge_type_8, 'L0_gnn_weight': _L0_gnn_in['weight'], 'L0_gnn_bias': _L0_gnn_in['bias'], 'L0_ffn_gate_w': _L0_ffn_in['gate_w'], 'L0_ffn_gate_b': _L0_ffn_in['gate_b'], 'L0_ffn_w1': _L0_ffn_in['w1'], 'L0_ffn_w2': _L0_ffn_in['w2'], 'L0_ffn_w3': _L0_ffn_in['w3']}

def reference(x, src, dst, edge_type_8, L0_gnn_weight, L0_gnn_bias, L0_ffn_gate_w, L0_ffn_gate_b, L0_ffn_w1, L0_ffn_w2, L0_ffn_w3):
    import jax
    import jax.numpy as jnp

    def _L0_gnn_ref(node_repr, weight, bias, edge_index, edge_types):
        import jax, jax.numpy as jnp
        import numpy as np
        NUM_NODES = 3125
        NUM_EDGES = 50000
        IN_DIM = 256
        OUT_DIM = 256
        NUM_RELATIONS = 8
        h_all = jnp.einsum('ni,roi->rno', node_repr, weight)
        src, dst = (edge_index[0], edge_index[1])
        msgs = h_all[edge_types, src]
        messages = jax.ops.segment_sum(msgs, dst, num_segments=node_repr.shape[0])
        return messages + bias

    def _L0_ffn_ref(x, gate_w, gate_b, w1, w2, w3):
        import jax, jax.numpy as jnp
        import numpy as np
        D_MODEL = 256
        N_EXPERTS = 16
        HIDDEN = 512
        SCALE = 0.02
        n_experts = w1.shape[0]
        logits = jnp.einsum('bsd,de->bse', x, gate_w) + gate_b
        probs = jax.nn.softmax(logits, axis=-1)
        top_probs, top_idx = jax.lax.top_k(probs, 2)
        top_probs = top_probs / jnp.sum(top_probs, axis=-1, keepdims=True)
        dispatch = jnp.sum(jax.nn.one_hot(top_idx, n_experts, dtype=x.dtype) * top_probs[..., None], axis=-2)
        h1 = jnp.einsum('bsd,edh->bseh', x, w1)
        h2 = jnp.einsum('bsd,edh->bseh', x, w2)
        hidden = jax.nn.silu(h1) * h2
        expert_out = jnp.einsum('bseh,eho->bseo', hidden, w3)
        return jnp.einsum('bseo,bse->bso', expert_out, dispatch)
    edge_index = jnp.stack([src, dst])
    x = x + _L0_gnn_ref(_layernorm(x, axis=-1), L0_gnn_weight, L0_gnn_bias, edge_index, edge_type_8)
    x = x + _L0_ffn_ref(_layernorm(x, axis=-1)[None], L0_ffn_gate_w, L0_ffn_gate_b, L0_ffn_w1, L0_ffn_w2, L0_ffn_w3)[0]
    return x

_drawn_inputs = setup_inputs


def setup_inputs(seed=0):
    import zlib

    import numpy as np

    out = dict(_drawn_inputs(seed))
    spreads = {'L0_gnn_bias': (0.0, 0.34), 'L0_ffn_gate_b': (0.0, 0.8)}
    factors = {'L0_ffn_gate_w': 8.0, 'L0_ffn_w1': 8.0, 'L0_ffn_w2': 8.0, 'L0_ffn_w3': 8.0}
    for name, (base, spread) in spreads.items():
        noise = np.random.default_rng([zlib.crc32(name.encode()), seed]).standard_normal(out[name].shape)
        drawn = base * np.exp(spread * noise) if base else spread * noise
        out[name] = jnp.asarray(drawn.astype(out[name].dtype))
    for name, factor in factors.items():
        out[name] = (out[name] * factor).astype(out[name].dtype)
    return out
```

```python
from contextlib import ExitStack

import concourse.bass as bass
from concourse import mybir

F32 = mybir.dt.float32
I32 = mybir.dt.int32
ALU = mybir.AluOpType
ACT = mybir.ActivationFunctionType
AX = mybir.AxisListType

P = 128
NODES, DIM, RELS = 3125, 256, 8
EDGES = 53125
EXPERTS, HIDDEN = 16, 512
EPS = 1e-5
KT = DIM // P
HT = HIDDEN // P
TILES = -(-NODES // P)
LAST = NODES - (TILES - 1) * P
CPG = 4
GE = CPG * P
GROUPS = -(-EDGES // GE)
TAIL = EDGES - (GROUPS - 1) * GE
FULL = (GROUPS - 1) // 16 * 16
RING = 4
ROUNDS = GROUPS // RING
WIN = 2
NO_NODE = 4095.0
ACC_TILES = TILES + WIN
RO = RELS * DIM
QW = 512
QUARTERS = RO // QW
PAIRS = 2 * NODES
SLOT_TILES = (PAIRS + EXPERTS * P) // P
SLOTS = SLOT_TILES * P
assert GROUPS % RING == 0 and SLOT_TILES % 2 == 0 and TILES % 2 == 1


def build(nc, x, src, dst, etype, w_rel, b_rel, gate_w, gate_b, w1, w2, w3, out):
    h_tab = nc.dram_tensor("h_tab", (TILES * P * RELS, DIM), F32, kind="Internal").ap()
    xs_tab = nc.dram_tensor("xs_tab", (SLOTS, DIM), F32, kind="Internal").ap()
    y_tab = nc.dram_tensor("y_tab", (SLOTS, DIM), F32, kind="Internal").ap()
    h_rows = h_tab.rearrange("(n r) o -> n (r o)", r=RELS)

    with ExitStack() as ctx:
        def sb(name, shape, dt=F32):
            return ctx.enter_context(nc.sbuf_tensor(name, shape, dt))

        def sem(name):
            return ctx.enter_context(nc.semaphore(name))

        ident = sb("ident", [P, P])
        ones = sb("ones", [P, P])
        before = sb("before", [P, P])
        iota_i = sb("iota_i", [P, WIN * P], I32)
        iota = sb("iota", [P, WIN * P])
        node_i = sb("node_i", [P, TILES], I32)
        x_sb = sb("x_sb", [P, TILES, DIM])
        acc = sb("acc", [P, ACC_TILES, DIM])
        bias = sb("bias", [P, DIM])
        stat = sb("stat", [P, TILES, 6])
        mean = sb("mean", [P, TILES])
        var = sb("var", [P, TILES])
        eps = sb("eps", [P, 1])
        dev = sb("dev", [P, TILES])
        rstd = sb("rstd", [P, TILES])
        xn = sb("xn", [P, 2, DIM])
        xT = sb("xT", [P, 2, KT, P])
        room = sb("room", [P, 4 * RO])
        w_raw = room[:, 0:2 * RO].rearrange("p (a i) -> p a i", i=DIM)
        wT = room[:, 2 * RO:4 * RO].rearrange("p (k n) -> p k n", k=KT)
        W12 = KT * HIDDEN
        W3 = HT * DIM
        w1_sb = [room[:, s * W12:(s + 1) * W12].rearrange("p (k n) -> p k n", k=KT) for s in range(2)]
        w2_sb = [room[:, (2 + s) * W12:(3 + s) * W12].rearrange("p (k n) -> p k n", k=KT) for s in range(2)]
        w3_sb = [room[:, 4 * W12 + s * W3:4 * W12 + (s + 1) * W3].rearrange("p (k n) -> p k n", k=HT) for s in range(2)]
        hb = sb("hb", [P, 2, RO])
        e_src = sb("e_src", [GROUPS, GE], I32)
        e_dst = sb("e_dst", [GROUPS, GE], I32)
        e_typ = sb("e_typ", [GROUPS, GE], I32)
        row_f = sb("row_f", [GROUPS, GE])
        dst_f = sb("dst_f", [GROUPS, GE])
        dst_m = sb("dst_m", [GROUPS, GE])
        ends = sb("ends", [GROUPS, 2])
        ends_i = sb("ends_i", [GROUPS, 2], I32)
        ends_t = sb("ends_t", [GROUPS, 2], I32)
        ends_f = sb("ends_f", [GROUPS, 2])
        win0 = sb("win0", [GROUPS, 1])
        gidx = sb("gidx", [P, (GROUPS + RING) * CPG], I32)
        drel = sb("drel", [P, GROUPS * CPG])
        lohi = sb("lohi", [1, 2, GROUPS])
        span = sb("span", [1, GROUPS])
        far = sb("far", [1, 1])
        far_i = sb("far_i", [1, 1], I32)
        far_h = sb("far_h", [1, 1], I32)
        n_pass = sb("n_pass", [1, 1], I32)
        tile_of = sb("tile_of", [1, GROUPS], I32)
        pass0 = sb("pass0", [P, 1])
        idx = sb("idx", [P, RING, CPG], I32)
        got = sb("got", [P, RING * CPG, DIM])
        hot = sb("hot", [P, 2, CPG, WIN * P])
        gw_sb = sb("gw_sb", [P, KT, EXPERTS])
        gb_sb = sb("gb_sb", [P, EXPERTS])
        TE = [P, TILES, EXPERTS]
        logit = sb("logit", TE)
        prob = sb("prob", TE)
        tmp = sb("tmp", TE)
        hot1 = sb("hot1", TE)
        hot2 = sb("hot2", TE)
        hots = sb("hots", TE)
        mtx = sb("mtx", [P, TILES])
        top = sb("top", [P, 2, TILES])
        pick = sb("pick", [P, TILES])
        wsum = sb("wsum", [P, TILES])
        wts = sb("wts", [P, 2, TILES])
        valid = sb("valid", [P, TILES])
        ET = [P, EXPERTS, TILES]
        tot = sb("tot", ET)
        carry = sb("carry", ET)
        incl = sb("incl", ET)
        base = sb("base", ET)
        n_tile = sb("n_tile", [P, EXPERTS])
        t_incl = sb("t_incl", [P, EXPERTS])
        t_off = sb("t_off", [P, EXPERTS])
        pos_f = sb("pos_f", [P, 2, TILES])
        pos = sb("pos", [P, 2, TILES], I32)
        own_edge = sb("own_edge", [P, TILES])
        own = sb("own", [1, SLOT_TILES, EXPERTS])
        own_f = sb("own_f", [1, SLOT_TILES])
        owner = sb("owner", [1, SLOT_TILES], I32)
        xs = sb("xs", [P, 2, DIM])
        xsT = sb("xsT", [P, 2, KT, P])
        gate = sb("gate", [P, 2, HIDDEN])
        hid = sb("hid", [P, 2, HIDDEN])
        hidT = sb("hidT", [P, 2, HT, P])
        y_sb = sb("y_sb", [P, 2, DIM])

        ps = ctx.enter_context(nc.psum_tensor("ps", [P, 8, QW], F32))

        pads_set = sem("pads_set")
        edges_in = sem("edges_in")
        w_in = sem("w_in")
        x_pad_set = sem("x_pad_set")
        x_in = sem("x_in")
        small_in = sem("small_in")
        pool_const = sem("pool_const")
        const_ready = sem("const_ready")
        iota_ready = sem("iota_ready")
        got_zero = sem("got_zero")
        xs_zeroed = sem("xs_zeroed")
        acc_init = sem("acc_init")
        vec_step = sem("vec_step")
        edge_rows = sem("edge_rows")
        edges_turned = sem("edges_turned")
        w_turned = sem("w_turned")
        wT_ready = sem("wT_ready")
        stats_raw = sem("stats_raw")
        stats_done = sem("stats_done")
        dev_done = sem("dev_done")
        rstd_done = sem("rstd_done")
        xn_ready = sem("xn_ready")
        x_turned = sem("x_turned")
        xT_ready = sem("xT_ready")
        h_done = sem("h_done")
        h_out_act = sem("h_out_act")
        h_out_vec = sem("h_out_vec")
        h_stored = [sem(f"h_stored{s}") for s in range(2)]
        pass_ready = sem("pass_ready")
        idx_ready = sem("idx_ready")
        gathered = [sem(f"gathered{c}") for c in range(RING * CPG)]
        hot_ready = sem("hot_ready")
        group_done = sem("group_done")
        acc_added = sem("acc_added")
        sums_done = sem("sums_done")
        gathers_begun = sem("gathers_begun")
        stats2_raw = sem("stats2_raw")
        stats2_done = sem("stats2_done")
        dev2_done = sem("dev2_done")
        rstd2_done = sem("rstd2_done")
        xn2_ready = sem("xn2_ready")
        xn2_copied = sem("xn2_copied")
        x2_turned = sem("x2_turned")
        x2T_ready = sem("x2T_ready")
        gate_done = sem("gate_done")
        logit_done = sem("logit_done")
        shift_done = sem("shift_done")
        exp_done = sem("exp_done")
        hots_done = sem("hots_done")
        ranks_done = sem("ranks_done")
        owner_done = sem("owner_done")
        pos_done = sem("pos_done")
        xs_scattered = sem("xs_scattered")
        xs_in = [sem(f"xs_in{s}") for s in range(2)]
        w12_in = [sem(f"w12_in{s}") for s in range(2)]
        w3_in = [sem(f"w3_in{s}") for s in range(2)]
        xs_turned = sem("xs_turned")
        xsT_ready = sem("xsT_ready")
        up_done = sem("up_done")
        gate_ready = sem("gate_ready")
        hid_ready = sem("hid_ready")
        hid_turned = sem("hid_turned")
        hidT_ready = sem("hidT_ready")
        y_done = sem("y_done")
        y_ready = sem("y_ready")
        y_stored = [sem(f"y_stored{s}") for s in range(2)]
        y_got = [sem(f"y_got{n}") for n in range(RING * CPG)]
        part_done = sem("part_done")
        out_ready = sem("out_ready")
        out_stored = sem("out_stored")

        block = ctx.enter_context(nc.Block())
        H_BANK = 0
        T_BANK = 4

        def bc(ap, shape, axis):
            return ap.unsqueeze(axis).to_broadcast(shape)

        @block.sync
        def _(sp):
            sp.wait_ge(pads_set, 1)
            for hbm, rows in ((src, e_src), (dst, e_dst), (etype, e_typ)):
                by_row = hbm[0:(GROUPS - 1) * GE].rearrange("(q e) -> q e", e=GE)
                sp.dma_start(rows[0:FULL, :], by_row[0:FULL, :]).then_inc(edges_in, 16)
                sp.dma_start(rows[FULL:GROUPS - 1, :], by_row[FULL:GROUPS - 1, :]).then_inc(edges_in, 16)
                sp.dma_start(rows[GROUPS - 1:GROUPS, 0:TAIL],
                             hbm[(GROUPS - 1) * GE:EDGES].rearrange("(a e) -> a e", a=1)).then_inc(edges_in, 16)
            sp.wait_ge(x_pad_set, 1)
            sp.dma_start(x_sb[:, 0:TILES - 1, :],
                         x[0:(TILES - 1) * P, :].rearrange("(t p) d -> p t d", p=P)).then_inc(x_in, 16)
            sp.dma_start(x_sb[0:LAST, TILES - 1, :], x[(TILES - 1) * P:NODES, :]).then_inc(x_in, 16)
            sp.dma_start(w_raw, w_rel.rearrange("r (a p) i -> p (r a) i", p=P)).then_inc(w_in, 16)
            sp.dma_start(bias[:, :], b_rel.rearrange("(a d) -> a d", a=1).to_broadcast([P, DIM])).then_inc(small_in, 16)
            sp.dma_start(gw_sb[:, :, :], gate_w.rearrange("(k p) e -> p k e", p=P)).then_inc(small_in, 16)
            sp.dma_start(gb_sb[:, :], gate_b.rearrange("(a d) -> a d", a=1).to_broadcast([P, EXPERTS])).then_inc(small_in, 16)
            sp.wait_ge(got_zero, 1)
            zw = RING * CPG
            for z in range(SLOT_TILES // zw):
                sp.dma_start(xs_tab[z * zw * P:(z + 1) * zw * P, :].rearrange("(t p) d -> p t d", p=P),
                             got[:, :, :]).then_inc(xs_zeroed, 16)

            def store_h(i, s):
                t = i * 2 + s
                sp.wait_ge(h_out_act, t * 2 + 2)
                sp.wait_ge(h_out_vec, t * 2 + 2)
                sp.dma_start(h_rows[bass.ds(t * P, P), :], hb[:, s, :]).then_inc(h_stored[s], 16)

            with sp.Fori(0, TILES // 2) as i:
                for s in range(2):
                    store_h(i, s)
            store_h(TILES // 2, 0)

            def load_xs(j, s):
                sp.dma_start(xs[:, s, :], xs_tab[bass.ds(j * P, P), :]).then_inc(xs_in[s], 16)

            def owner_of(j):
                return sp.value_load(owner[0:1, bass.ds(j, 1)], min_val=0, max_val=EXPERTS - 1)

            def load_w12(j, s, used=None):
                e = owner_of(j)
                if used is not None:
                    sp.wait_ge(up_done, used)
                for w, room_s in ((w1, w1_sb[s]), (w2, w2_sb[s])):
                    sp.dma_start(room_s, w[bass.ds(e, 1), :, :].rearrange("a (k p) n -> p (a k) n", p=P)).then_inc(w12_in[s], 16)

            def load_w3(j, s, used=None):
                e = owner_of(j)
                if used is not None:
                    sp.wait_ge(y_done, used)
                sp.dma_start(w3_sb[s], w3[bass.ds(e, 1), :, :].rearrange("a (k p) n -> p (a k) n", p=P)).then_inc(w3_in[s], 16)

            def store_y(j, s):
                sp.wait_ge(y_ready, j + 1)
                sp.dma_start(y_tab[bass.ds(j * P, P), :], y_sb[:, s, :]).then_inc(y_stored[s], 16)

            def expert_tile(j, s, first=False, more=True, last=False):
                if more:
                    load_w12(j + 2, s, used=j + 1)
                    sp.wait_ge(xs_turned, j + 1)
                    load_xs(j + 2, s)
                if not first:
                    store_y(j - 1, 1 - s)
                    if not last:
                        load_w3(j + 1, 1 - s, used=j + 1)

            sp.wait_ge(owner_done, 1)
            for s in range(2):
                load_w12(s, s)
                load_w3(s, s)
            sp.wait_ge(xs_scattered, 2 * TILES * 16)
            for s in range(2):
                load_xs(s, s)
            expert_tile(0, 0, first=True)
            expert_tile(1, 1)
            with sp.Fori(1, SLOT_TILES // 2 - 1) as i:
                for s in range(2):
                    expert_tile(i * 2 + s, s)
            expert_tile(SLOT_TILES - 2, 0, more=False)
            expert_tile(SLOT_TILES - 1, 1, more=False, last=True)
            store_y(SLOT_TILES - 1, 1)

            for t in range(TILES):
                rows = P if t < TILES - 1 else LAST
                sp.wait_ge(out_ready, t + 1)
                sp.dma_start(out[t * P:t * P + rows, :], acc[0:rows, t, :]).then_inc(out_stored, 16)
            sp.wait_ge(out_stored, TILES * 16)

        @block.gpsimd
        def _(pool):
            nc.gpsimd.memset(ident[:, :], 0.0).then_inc(pool_const, 1)
            nc.gpsimd.memset(ones[:, :], 1.0).then_inc(pool_const, 1)
            pool.wait_ge(pool_const, 2)
            nc.gpsimd.affine_select(out=ident[:, :], in_=ident[:, :], compare_op=ALU.not_equal, fill=1.0, base=0,
                                    pattern=[[-1, P]], channel_multiplier=1).then_inc(const_ready, 1)
            nc.gpsimd.affine_select(out=before[:, :], in_=ones[:, :], compare_op=ALU.is_gt, fill=0.0, base=0,
                                    pattern=[[1, P]], channel_multiplier=-1).then_inc(const_ready, 1)
            nc.gpsimd.iota(iota_i[:, :], pattern=[[1, WIN * P]], base=0, channel_multiplier=0).then_inc(iota_ready, 1)
            nc.gpsimd.iota(node_i[:, :], pattern=[[P, TILES]], base=0, channel_multiplier=1).then_inc(iota_ready, 1)
            nc.gpsimd.memset(got[:, :, :], 0.0).then_inc(got_zero, 1)
            nc.gpsimd.memset(acc[:, TILES:ACC_TILES, :], 0.0).then_inc(acc_init, 1)
            pool.wait_ge(x_in, 32)
            pool.wait_ge(small_in, 48)
            nc.gpsimd.tensor_tensor(acc[:, 0:TILES, :], x_sb[:, :, :], bc(bias[:, :], [P, TILES, DIM], 1),
                                    ALU.add).then_inc(acc_init, 1)

            pool.wait_ge(xs_zeroed, SLOT_TILES // (RING * CPG) * 16)
            pool.wait_ge(h_stored[0], (TILES + 1) // 2 * 16)
            pool.wait_ge(h_stored[1], TILES // 2 * 16)
            pool.wait_ge(pass_ready, 2)
            passes = pool.value_load(n_pass[0:1, 0:1], min_val=1, max_val=TILES)
            with pool.Fori(0, passes) as p:
                with pool.Fori(0, ROUNDS) as i:
                    for g in range(RING):
                        pool.wait_ge(idx_ready, p * GROUPS + i * RING + g + 1)
                        pool.sem_inc(gathers_begun, 1)
                        for c in range(CPG):
                            n = g * CPG + c
                            nc.gpsimd.indirect_dma_start(
                                got[:, n, :], None, h_tab,
                                bass.IndirectOffsetOnAxis(ap=idx[:, g, c:c + 1], axis=0)).then_inc(gathered[n], 16)

            pool.wait_ge(pos_done, 1)
            for t in range(TILES):
                rows = P if t < TILES - 1 else LAST
                for k in range(2):
                    nc.gpsimd.indirect_dma_start(
                        xs_tab, bass.IndirectOffsetOnAxis(ap=pos[0:rows, k, t:t + 1], axis=0),
                        x_sb[0:rows, t, :], None).then_inc(xs_scattered, 16)

            for s in range(2):
                pool.wait_ge(y_stored[s], SLOT_TILES // 2 * 16)
            ring = RING * CPG // 2
            for t in range(TILES):
                rows = P if t < TILES - 1 else LAST
                if t >= ring:
                    pool.wait_ge(out_ready, t - ring + 1)
                for k in range(2):
                    n = t % ring * 2 + k
                    nc.gpsimd.indirect_dma_start(
                        got[0:rows, n, :], None, y_tab,
                        bass.IndirectOffsetOnAxis(ap=pos[0:rows, k, t:t + 1], axis=0)).then_inc(y_got[n], 16)

        @block.scalar
        def _(act):
            act.wait_ge(stats_done, 1)
            nc.scalar.activation(dev[:, :], var[:, :], ACT.Sqrt, bias=eps[:, 0:1]).then_inc(dev_done, 1)
            for n in range(8):
                k, rp = n // 4, n % 4
                act.wait_ge(w_turned, n + 1)
                nc.scalar.copy(wT[:, k, rp * QW:(rp + 1) * QW], ps[:, n, :]).then_inc(wT_ready, 1)

            def copy_xT(t, s):
                act.wait_ge(x_turned, t + 1)
                nc.scalar.copy(xT[:, s, :, :], ps[:, T_BANK + s, 0:DIM].rearrange("p (k n) -> p k n", k=KT)).then_inc(xT_ready, 1)

            def message_tile(i, s, ahead=True):
                t = i * 2 + s
                if ahead:
                    act.wait_ge(h_done, t * QUARTERS)
                    copy_xT(t + 1, 1 - s)
                act.wait_ge(h_stored[s], i * 16)
                for q in range(2):
                    act.wait_ge(h_done, t * QUARTERS + q + 1)
                    nc.scalar.copy(hb[:, s, q * QW:(q + 1) * QW], ps[:, H_BANK + q, :]).then_inc(h_out_act, 1)

            copy_xT(0, 0)
            with act.Fori(0, TILES // 2) as i:
                for s in range(2):
                    message_tile(i, s)
            message_tile(TILES // 2, 0, ahead=False)

            act.wait_ge(stats2_done, 1)
            nc.scalar.activation(dev[:, :], var[:, :], ACT.Sqrt, bias=eps[:, 0:1]).then_inc(dev2_done, 1)

            def route_tile(i, s):
                t = i * 2 + s
                act.wait_ge(xn2_ready, t + 1)
                act.wait_ge(x2_turned, t)
                nc.scalar.copy(xn[:, s, :], x_sb[:, bass.ds(t, 1), :].rearrange("p a d -> p (a d)")).then_inc(xn2_copied, 1)
                act.wait_ge(x2_turned, t + 2)
                act.wait_ge(gate_done, t)
                nc.scalar.copy(xT[:, s, :, :], ps[:, T_BANK + s, 0:DIM].rearrange("p (k n) -> p k n", k=KT)).then_inc(x2T_ready, 1)

            with act.Fori(0, TILES // 2) as i:
                for s in range(2):
                    route_tile(i, s)
            route_tile(TILES // 2, 0)
            act.wait_ge(shift_done, 1)
            nc.scalar.activation(prob[:, :, :], logit[:, :, :], ACT.Exp).then_inc(exp_done, 1)

            def copy_xsT(j, s):
                act.wait_ge(xs_turned, j + 1)
                nc.scalar.copy(xsT[:, s, :, :], ps[:, 4, 0:DIM].rearrange("p (k n) -> p k n", k=KT)).then_inc(xsT_ready, 1)

            def expert_tile(j, s, last=False):
                act.wait_ge(up_done, j + 1)
                act.wait_ge(hid_ready, j)
                nc.scalar.activation(gate[:, s, :], ps[:, s, :], ACT.Silu).then_inc(gate_ready, 1)
                if not last:
                    copy_xsT(j + 1, 1 - s)
                act.wait_ge(hid_turned, j + 2)
                act.wait_ge(y_done, j)
                nc.scalar.copy(hidT[:, s, :, :], ps[:, 5, :].rearrange("p (k n) -> p k n", k=HT)).then_inc(hidT_ready, 1)

            copy_xsT(0, 0)
            with act.Fori(0, SLOT_TILES // 2 - 1) as i:
                for s in range(2):
                    expert_tile(i * 2 + s, s)
            expert_tile(SLOT_TILES - 2, 0)
            expert_tile(SLOT_TILES - 1, 1, last=True)

        @block.vector
        def _(dve):
            steps = [0]

            def step(ins):
                steps[0] += 1
                ins.then_inc(vec_step, 1)
                dve.wait_ge(vec_step, steps[0])

            dve.sem_inc(acc_added, 1)
            dve.sem_inc(logit_done, 1)
            dve.sem_inc(hid_ready, 1)

            def mean_and_var(done):
                v.tensor_tensor(mean[:, :], stat[:, :, 1], stat[:, :, 4], ALU.add)
                v.tensor_tensor(var[:, :], stat[:, :, 2], stat[:, :, 5], ALU.add)
                step(v.tensor_tensor(dev[:, :], stat[:, :, 1], stat[:, :, 4], ALU.subtract))
                v.tensor_scalar(mean[:, :], mean[:, :], 0.5, None, ALU.mult)
                step(v.scalar_tensor_tensor(out=dev[:, :], in0=dev[:, :], scalar=0.25, in1=dev[:, :],
                                            op0=ALU.mult, op1=ALU.mult))
                v.scalar_tensor_tensor(out=var[:, :], in0=var[:, :], scalar=1.0 / DIM, in1=dev[:, :],
                                       op0=ALU.mult, op1=ALU.add).then_inc(done, 1)

            v = nc.vector
            v.memset(e_src[:, :], 0)
            v.memset(e_typ[:, :], 0)
            v.memset(e_dst[:, :], int(NO_NODE)).then_inc(pads_set, 1)
            v.memset(x_sb[:, TILES - 1, :], 0.0).then_inc(x_pad_set, 1)
            dve.wait_ge(iota_ready, 2)
            step(v.tensor_copy(iota[:, :], iota_i[:, :]))
            step(v.tensor_copy(pick[:, :], node_i[:, :]))
            step(v.tensor_scalar(valid[:, :], pick[:, :], float(NODES), None, ALU.is_lt))
            v.memset(eps[:, :], EPS)
            v.memset(pass0[:, :], 0.0)
            v.memset(carry[:, :, :], 1.0)

            dve.wait_ge(edges_in, 9 * 16)
            v.scalar_tensor_tensor(out=row_f[:, :], in0=e_src[:, :], scalar=float(RELS), in1=e_typ[:, :],
                                   op0=ALU.mult, op1=ALU.add)
            step(v.tensor_copy(dst_f[:, :], e_dst[:, :]))
            step(v.scalar_tensor_tensor(out=dst_m[:, :], in0=dst_f[:, :], scalar=NO_NODE, in1=dst_f[:, :],
                                        op0=ALU.is_lt, op1=ALU.mult))
            v.tensor_reduce(ends[:, 0:1], dst_f[:, :], AX.X, ALU.min)
            step(v.tensor_reduce(ends[:, 1:2], dst_m[:, :], AX.X, ALU.max))
            step(v.tensor_copy(ends_i[:, :], ends[:, :]))
            step(v.tensor_scalar(ends_t[:, :], ends_i[:, :], P.bit_length() - 1, None, ALU.logical_shift_right))
            step(v.tensor_copy(ends_f[:, :], ends_t[:, :]))
            step(v.tensor_scalar(win0[:, :], ends_f[:, 0:1], float(P), None, ALU.mult))
            v.tensor_scalar(dst_m[:, :], dst_f[:, :], win0[:, 0:1], None, ALU.subtract).then_inc(edge_rows, 1)

            dve.wait_ge(x_in, 32)
            with dve.Fori(0, TILES) as t:
                v.bn_stats(stat[:, bass.ds(t, 1), :].rearrange("p a c -> p (a c)"),
                           x_sb[:, bass.ds(t, 1), :].rearrange("p a d -> p (a d)")).then_inc(stats_raw, 1)
            dve.wait_ge(stats_raw, TILES)
            mean_and_var(stats_done)

            dve.wait_ge(edges_turned, 1)
            in_row = gidx[:, 0:GROUPS * CPG].rearrange("p (q c) -> p c q", c=CPG)
            step(v.tensor_copy(in_row, ps[:, 5, 0:GROUPS * CPG].rearrange("p (c q) -> p c q", c=CPG)))
            v.tensor_copy(gidx[:, GROUPS * CPG:(GROUPS + RING) * CPG], gidx[:, 0:RING * CPG])
            step(v.tensor_copy(drel[:, :].rearrange("p (q c) -> p c q", c=CPG),
                               ps[:, 6, 0:GROUPS * CPG].rearrange("p (c q) -> p c q", c=CPG)))
            step(v.tensor_copy(lohi[:, :, :], ps[0:1, 7, 0:2 * GROUPS].rearrange("p (c q) -> p c q", c=2)))
            step(v.tensor_tensor(span[:, :], lohi[:, 1, :], lohi[:, 0, :], ALU.subtract))
            step(v.tensor_reduce(far[:, :], span[:, :], AX.X, ALU.max))
            step(v.tensor_copy(far_i[:, :], far[:, :]))
            step(v.tensor_scalar(far_h[:, :], far_i[:, :], WIN.bit_length() - 1, None, ALU.logical_shift_right))
            v.tensor_scalar(n_pass[:, :], far_h[:, :], 1, None, ALU.add).then_inc(pass_ready, 1)
            v.tensor_copy(tile_of[:, :], lohi[:, 0, :]).then_inc(pass_ready, 1)
            v.tensor_copy(idx[:, :, :], gidx[:, 0:RING * CPG].rearrange("p (g c) -> p g c", c=CPG)).then_inc(idx_ready, RING)

            dve.wait_ge(dev_done, 1)
            v.reciprocal(rstd[:, :], dev[:, :]).then_inc(rstd_done, 1)
            dve.wait_ge(rstd_done, 1)

            def normalize(t, s):
                v.tensor_scalar(xn[:, s, :], x_sb[:, bass.ds(t, 1), :].rearrange("p a d -> p (a d)"),
                                mean[:, bass.ds(t, 1)],
                                rstd[:, bass.ds(t, 1)], ALU.subtract, ALU.mult).then_inc(xn_ready, 1)

            def message_tile(i, s, ahead=True):
                t = i * 2 + s
                if ahead:
                    dve.wait_ge(x_turned, t + 1)
                    normalize(t + 2, s)
                dve.wait_ge(h_stored[s], i * 16)
                for q in range(2, QUARTERS):
                    dve.wait_ge(h_done, t * QUARTERS + q + 1)
                    v.tensor_copy(hb[:, s, q * QW:(q + 1) * QW], ps[:, H_BANK + q, :]).then_inc(h_out_vec, 1)

            normalize(0, 0)
            normalize(1, 1)
            with dve.Fori(0, TILES // 2 - 1) as i:
                for s in range(2):
                    message_tile(i, s)
            message_tile(TILES // 2 - 1, 0)
            message_tile(TILES // 2 - 1, 1, ahead=False)
            message_tile(TILES // 2, 0, ahead=False)

            def one_hots(p, g, s):
                for c in range(CPG):
                    v.tensor_scalar(hot[:, s, c, :], iota[:, :], pass0[:, 0:1], drel[:, bass.ds(g * CPG + c, 1)],
                                    ALU.add, ALU.is_equal).then_inc(hot_ready, 1)

            def add_group(p, i, r):
                g = i * RING + r
                n = p * GROUPS + g
                s = r % 2
                first = dve.value_load(tile_of[0:1, bass.ds(g, 1)], min_val=0, max_val=TILES)
                dve.wait_ge(group_done, n + 1)
                dve.wait_ge(acc_added, n + 1)
                window = acc[:, bass.ds(first, WIN), :]
                v.tensor_tensor(window, window, ps[:, WIN * s:WIN * (s + 1), 0:DIM], ALU.add).then_inc(acc_added, 1)
                v.tensor_copy(idx[:, r, :], gidx[:, bass.ds((g + RING) * CPG, CPG)]).then_inc(idx_ready, 1)

            dve.wait_ge(pass_ready, 2)
            dve.wait_ge(acc_init, 2)
            passes = dve.value_load(n_pass[0:1, 0:1], min_val=1, max_val=TILES)
            with dve.Fori(0, passes) as p:
                one_hots(p, 0, 0)
                with dve.Fori(0, ROUNDS - 1) as i:
                    for r in range(RING):
                        one_hots(p, i * RING + r + 1, (r + 1) % 2)
                        add_group(p, i, r)
                for r in range(RING):
                    if r < RING - 1:
                        one_hots(p, (ROUNDS - 1) * RING + r + 1, (r + 1) % 2)
                    add_group(p, ROUNDS - 1, r)
                v.tensor_scalar(pass0[:, :], pass0[:, :], float(WIN * P), None, ALU.add).then_inc(pass_ready, 1)
                v.tensor_scalar(tile_of[:, :], tile_of[:, :], WIN, TILES, ALU.add, ALU.min).then_inc(pass_ready, 1)
                dve.wait_ge(pass_ready, p * 2 + 4)
            dve.wait_ge(acc_added, passes * GROUPS + 1)
            v.memset(pass0[:, :], 0.0).then_inc(sums_done, 1)
            dve.wait_ge(sums_done, 1)

            with dve.Fori(0, TILES) as t:
                v.bn_stats(stat[:, bass.ds(t, 1), :].rearrange("p a c -> p (a c)"),
                           acc[:, bass.ds(t, 1), :].rearrange("p a d -> p (a d)")).then_inc(stats2_raw, 1)
            dve.wait_ge(stats2_raw, TILES)
            mean_and_var(stats2_done)
            dve.wait_ge(dev2_done, 1)
            v.reciprocal(rstd[:, :], dev[:, :]).then_inc(rstd2_done, 1)
            dve.wait_ge(rstd2_done, 1)
            with dve.Fori(0, TILES) as t:
                v.tensor_scalar(x_sb[:, bass.ds(t, 1), :].rearrange("p a d -> p (a d)"),
                                acc[:, bass.ds(t, 1), :].rearrange("p a d -> p (a d)"),
                                mean[:, bass.ds(t, 1)],
                                rstd[:, bass.ds(t, 1)], ALU.subtract, ALU.mult).then_inc(xn2_ready, 1)

            def gate_bias(i, s):
                t = i * 2 + s
                dve.wait_ge(gate_done, t + 2)
                v.tensor_tensor(logit[:, bass.ds(t, 1), :].rearrange("p a e -> p (a e)"), ps[:, 6 + s, 0:EXPERTS],
                                gb_sb[:, :], ALU.add).then_inc(logit_done, 1)

            with dve.Fori(0, TILES // 2) as i:
                for s in range(2):
                    gate_bias(i, s)
            gate_bias(TILES // 2, 0)

            dve.wait_ge(logit_done, TILES + 1)
            step(v.tensor_reduce(mtx[:, :], logit[:, :, :], AX.X, ALU.max))
            v.tensor_tensor(logit[:, :, :], logit[:, :, :], bc(mtx[:, :], TE, 2), ALU.subtract).then_inc(shift_done, 1)
            dve.wait_ge(exp_done, 1)
            step(v.tensor_reduce(mtx[:, :], prob[:, :, :], AX.X, ALU.add))
            step(v.reciprocal(wsum[:, :], mtx[:, :]))
            step(v.tensor_tensor(prob[:, :, :], prob[:, :, :], bc(wsum[:, :], TE, 2), ALU.mult))

            e_iota = bc(iota[:, 0:EXPERTS], TE, 1)

            def best(k, hot_k):
                step(v.tensor_reduce(top[:, k, :], prob[:, :, :], AX.X, ALU.max))
                step(v.tensor_tensor(tmp[:, :, :], prob[:, :, :], bc(top[:, k, :], TE, 2), ALU.is_lt))
                step(v.scalar_tensor_tensor(out=tmp[:, :, :], in0=tmp[:, :, :], scalar=float(EXPERTS), in1=e_iota,
                                            op0=ALU.mult, op1=ALU.add))
                step(v.tensor_reduce(pick[:, :], tmp[:, :, :], AX.X, ALU.min))
                step(v.tensor_tensor(hot_k[:, :, :], e_iota, bc(pick[:, :], TE, 2), ALU.is_equal))

            best(0, hot1)
            step(v.scalar_tensor_tensor(out=prob[:, :, :], in0=hot1[:, :, :], scalar=-2.0, in1=prob[:, :, :],
                                        op0=ALU.mult, op1=ALU.add))
            best(1, hot2)
            step(v.tensor_tensor(wsum[:, :], top[:, 0, :], top[:, 1, :], ALU.add))
            step(v.reciprocal(mtx[:, :], wsum[:, :]))
            step(v.tensor_tensor(wts[:, :, :], top[:, :, :], bc(mtx[:, :], [P, 2, TILES], 1), ALU.mult))

            v.tensor_tensor(hot1[:, :, :], hot1[:, :, :], bc(valid[:, :], TE, 2), ALU.mult)
            step(v.tensor_tensor(hot2[:, :, :], hot2[:, :, :], bc(valid[:, :], TE, 2), ALU.mult))
            v.tensor_tensor(hots[:, :, :], hot1[:, :, :], hot2[:, :, :], ALU.add).then_inc(hots_done, 1)
            v.memset(carry[:, :, 0:1], 0.0)
            dve.wait_ge(ranks_done, 2)
            step(v.tensor_copy(tot[:, :, :], ps[:, 1, 0:TILES * EXPERTS].rearrange("p (t e) -> p e t", e=EXPERTS)))
            flat = "p e t -> p (e t)"
            step(v.tensor_tensor_scan(incl[:, :, :].rearrange(flat), carry[:, :, :].rearrange(flat),
                                      tot[:, :, :].rearrange(flat), 0.0, ALU.mult, ALU.add))
            v.tensor_scalar(own_edge[:, :], iota[:, 0:TILES], float(P), None, ALU.mult)
            step(v.tensor_tensor(base[:, :, :], incl[:, :, :], tot[:, :, :], ALU.subtract))
            step(v.tensor_tensor(tot[:, :, :], bc(incl[:, :, TILES - 1], ET, 2), bc(own_edge[:, :], ET, 1), ALU.is_gt))
            step(v.tensor_reduce(n_tile[:, :], tot[:, :, :], AX.X, ALU.add))
            step(v.tensor_scalar(n_tile[:, :], n_tile[:, :], 1.0, None, ALU.max))
            step(v.tensor_tensor_scan(t_incl[:, :], ones[:, 0:EXPERTS], n_tile[:, :], 0.0, ALU.mult, ALU.add))
            step(v.tensor_tensor(t_off[:, :], t_incl[:, :], n_tile[:, :], ALU.subtract))
            OW = [1, SLOT_TILES, EXPERTS]
            step(v.tensor_tensor(own[:, :, :], bc(iota[0:1, 0:SLOT_TILES], OW, 2), bc(t_off[0:1, :], OW, 1), ALU.is_ge))
            step(v.tensor_reduce(own_f[:, :], own[:, :, :], AX.X, ALU.add))
            v.tensor_scalar(owner[:, :], own_f[:, :], -1.0, None, ALU.add).then_inc(owner_done, 1)
            step(v.scalar_tensor_tensor(out=base[:, :, :], in0=bc(t_off[:, :], ET, 2), scalar=float(P), in1=base[:, :, :],
                                        op0=ALU.mult, op1=ALU.add))
            step(v.tensor_tensor(tmp[:, :, :], ps[:, 0, 0:TILES * EXPERTS].rearrange("p (t e) -> p t e", e=EXPERTS),
                                 base[:, :, :].rearrange("p e t -> p t e"), ALU.add))
            v.tensor_tensor(hot1[:, :, :], hot1[:, :, :], tmp[:, :, :], ALU.mult)
            step(v.tensor_tensor(hot2[:, :, :], hot2[:, :, :], tmp[:, :, :], ALU.mult))
            v.tensor_reduce(pos_f[:, 0, :], hot1[:, :, :], AX.X, ALU.add)
            step(v.tensor_reduce(pos_f[:, 1, :], hot2[:, :, :], AX.X, ALU.add))
            v.tensor_copy(pos[:, :, :], pos_f[:, :, :]).then_inc(pos_done, 1)

            def copy_y(j, s, i):
                dve.wait_ge(y_done, j + 2)
                dve.wait_ge(y_stored[s], i * 16)
                v.tensor_copy(y_sb[:, s, :], ps[:, 6 + s, 0:DIM]).then_inc(y_ready, 1)

            def expert_tile(i, s, first=False):
                j = i * 2 + s
                dve.wait_ge(gate_ready, j + 1)
                dve.wait_ge(hid_turned, j)
                v.tensor_tensor(hid[:, s, :], gate[:, s, :], ps[:, 2 + s, :], ALU.mult).then_inc(hid_ready, 1)
                if not first:
                    copy_y(j - 1, 1 - s, i if s == 1 else i - 1)

            expert_tile(0, 0, first=True)
            expert_tile(0, 1)
            with dve.Fori(1, SLOT_TILES // 2) as i:
                for s in range(2):
                    expert_tile(i, s)
            copy_y(SLOT_TILES - 1, 1, SLOT_TILES // 2 - 1)

            ring = RING * CPG // 2
            for t in range(TILES):
                rows = P if t < TILES - 1 else LAST
                for k in range(2):
                    n = t % ring * 2 + k
                    dve.wait_ge(y_got[n], (t // ring + 1) * 16)
                    if k:
                        dve.wait_ge(part_done, t + 1)
                    v.scalar_tensor_tensor(out=acc[0:rows, t, :], in0=got[0:rows, n, :], scalar=wts[0:rows, k, t:t + 1],
                                           in1=acc[0:rows, t, :], op0=ALU.mult, op1=ALU.add
                                           ).then_inc(out_ready if k else part_done, 1)

        @block.tensor
        def _(pe):
            pe.sem_inc(x2_turned, 1)
            pe.sem_inc(gate_done, 1)
            pe.sem_inc(hid_turned, 1)
            pe.sem_inc(y_done, 1)

            mm = nc.tensor.matmul
            pe.wait_ge(const_ready, 2)
            pe.wait_ge(edge_rows, 1)
            for bank, rows in ((5, row_f), (6, dst_m)):
                for c in range(CPG):
                    nc.tensor.transpose(ps[:, bank, c * GROUPS:(c + 1) * GROUPS], rows[:, c * P:(c + 1) * P],
                                        ident[0:GROUPS, 0:GROUPS])
            for c in range(2):
                last = nc.tensor.transpose(ps[0:1, 7, c * GROUPS:(c + 1) * GROUPS], ends_f[:, c:c + 1],
                                           ident[0:GROUPS, 0:GROUPS])
            last.then_inc(edges_turned, 1)

            pe.wait_ge(w_in, 16)
            pe.wait_ge(pass_ready, 2)
            pe.wait_ge(idx_ready, RING)
            for n in range(8):
                k, rp = n // 4, n % 4
                for a in range(4):
                    last = nc.tensor.transpose(ps[:, n, a * P:(a + 1) * P], w_raw[:, rp * 4 + a, k * P:(k + 1) * P], ident[:, :])
                last.then_inc(w_turned, 1)

            def turn_x(t, s):
                pe.wait_ge(xn_ready, t + 1)
                for k in range(KT):
                    last = nc.tensor.transpose(ps[:, T_BANK + s, k * P:(k + 1) * P], xn[:, s, k * P:(k + 1) * P], ident[:, :])
                last.then_inc(x_turned, 1)

            def message_tile(i, s, ahead=True):
                t = i * 2 + s
                pe.wait_ge(xT_ready, t + 1)
                if ahead:
                    turn_x(t + 1, 1 - s)
                for q in range(QUARTERS):
                    if q % 2 == 0:
                        pe.wait_ge(h_out_act if q < 2 else h_out_vec, t * 2)
                    for k in range(KT):
                        last = mm(ps[:, H_BANK + q, :], xT[:, s, k, :], wT[:, k, q * QW:(q + 1) * QW],
                                  start=(k == 0), stop=(k == KT - 1))
                    last.then_inc(h_done, 1)

            pe.wait_ge(wT_ready, 8)
            turn_x(0, 0)
            with pe.Fori(0, TILES // 2) as i:
                for s in range(2):
                    message_tile(i, s)
            message_tile(TILES // 2, 0, ahead=False)

            pe.wait_ge(h_out_act, TILES * 2)
            pe.wait_ge(h_out_vec, TILES * 2)
            passes = pe.value_load(n_pass[0:1, 0:1], min_val=1, max_val=TILES)
            with pe.Fori(0, passes) as p:
                with pe.Fori(0, ROUNDS) as i:
                    for r in range(RING):
                        n = p * GROUPS + i * RING + r
                        pe.wait_ge(acc_added, n)
                        for c in range(CPG):
                            pe.wait_ge(hot_ready, n * CPG + c + 1)
                            pe.wait_ge(gathered[r * CPG + c], (p * ROUNDS + i + 1) * 16)
                            for w in range(WIN):
                                last = mm(ps[:, WIN * (r % 2) + w, 0:DIM], hot[:, r % 2, c, w * P:(w + 1) * P],
                                          got[:, r * CPG + c, :], start=(c == 0), stop=(c == CPG - 1))
                        last.then_inc(group_done, 1)

            def route_tile(i, s):
                t = i * 2 + s
                pe.wait_ge(xn2_copied, t + 1)
                pe.wait_ge(x2T_ready, t)
                for k in range(KT):
                    last = nc.tensor.transpose(ps[:, T_BANK + s, k * P:(k + 1) * P], xn[:, s, k * P:(k + 1) * P], ident[:, :])
                last.then_inc(x2_turned, 1)
                pe.wait_ge(x2T_ready, t + 1)
                pe.wait_ge(logit_done, t)
                for k in range(KT):
                    last = mm(ps[:, 6 + s, 0:EXPERTS], xT[:, s, k, :], gw_sb[:, k, :], start=(k == 0), stop=(k == KT - 1))
                last.then_inc(gate_done, 1)

            with pe.Fori(0, TILES // 2) as i:
                for s in range(2):
                    route_tile(i, s)
            route_tile(TILES // 2, 0)

            pe.wait_ge(hots_done, 1)
            flat = hots[:, :, :].rearrange("p t e -> p (t e)")
            for bank, lhs in ((0, before), (1, ones)):
                mm(ps[:, bank, 0:TILES * EXPERTS], lhs[:, :], flat, start=True, stop=True).then_inc(ranks_done, 1)
            pe.wait_ge(pos_done, 1)

            def turn_xs(j, s, i):
                pe.wait_ge(xs_in[s], (i + 1) * 16)
                for k in range(KT):
                    last = nc.tensor.transpose(ps[:, 4, k * P:(k + 1) * P], xs[:, s, k * P:(k + 1) * P], ident[:, :])
                last.then_inc(xs_turned, 1)

            def down(j, s, i):
                pe.wait_ge(hidT_ready, j + 1)
                pe.wait_ge(w3_in[s], (i + 1) * 16)
                pe.wait_ge(y_ready, j - 1) if not isinstance(j, int) or j >= 2 else None
                for k in range(HT):
                    last = mm(ps[:, 6 + s, 0:DIM], hidT[:, s, k, :], w3_sb[s][:, k, :],
                              start=(k == 0), stop=(k == HT - 1))
                last.then_inc(y_done, 1)

            def expert_tile(i, s, first=False, last_tile=False):
                j = i * 2 + s
                pe.wait_ge(xsT_ready, j + 1)
                pe.wait_ge(w12_in[s], (i + 1) * 32)
                pe.wait_ge(hid_ready, j)
                for bank, w in ((s, w1_sb[s]), (2 + s, w2_sb[s])):
                    for k in range(KT):
                        last = mm(ps[:, bank, :], xsT[:, s, k, :], w[:, k, :], start=(k == 0), stop=(k == KT - 1))
                last.then_inc(up_done, 1)
                if not first:
                    down(j - 1, 1 - s, i if s == 1 else i - 1)
                if not last_tile:
                    turn_xs(j + 1, 1 - s, i if s == 0 else i + 1)
                pe.wait_ge(hid_ready, j + 2)
                for k in range(HT):
                    last = nc.tensor.transpose(ps[:, 5, k * P:(k + 1) * P], hid[:, s, k * P:(k + 1) * P], ident[:, :])
                last.then_inc(hid_turned, 1)

            turn_xs(0, 0, 0)
            half = SLOT_TILES // 2
            expert_tile(0, 0, first=True)
            expert_tile(0, 1)
            with pe.Fori(1, half - 1) as i:
                for s in range(2):
                    expert_tile(i, s)
            expert_tile(half - 1, 0)
            expert_tile(half - 1, 1, last_tile=True)
            down(SLOT_TILES - 1, 1, half - 1)


_INS = ["x", "src", "dst", "edge_type_8", "L0_gnn_weight", "L0_gnn_bias", "L0_ffn_gate_w", "L0_ffn_gate_b",
        "L0_ffn_w1", "L0_ffn_w2", "L0_ffn_w3"]


def kernel(**inputs):
    import numpy as np
    import concourse.bacc as bacc
    from concourse.bass_utils import run_bass_kernel_spmd

    nc = bacc.Bacc("TRN2", target_bir_lowering=False, num_devices=1)
    arrays, args = {}, []
    for name in _INS:
        a = np.ascontiguousarray(inputs[name])
        arrays[f"in_{name}"] = a
        args.append(nc.dram_tensor(f"in_{name}", a.shape, mybir.dt.from_np(a.dtype), kind="ExternalInput").ap())
    out = nc.dram_tensor("out", (NODES, DIM), F32, kind="ExternalOutput").ap()
    build(nc, *args, out)
    return run_bass_kernel_spmd(nc, [arrays], core_ids=[0]).results[0]["out"]
```
